# Optimizing a Trainium2 kernel written in Bass

```python
import numpy as np
import jax
import jax.numpy as jnp

def _softmax(x, axis=-1):
    return jax.nn.softmax(x, axis=axis)

def _gelu(x):
    return jax.nn.gelu(x, approximate=True)

def _silu(x):
    return jax.nn.silu(x)

def _sigmoid(x):
    return jax.nn.sigmoid(x)

def _layernorm(x, axis=-1, eps=1e-05):
    m = jnp.mean(x, axis=axis, keepdims=True)
    v = jnp.var(x, axis=axis, keepdims=True)
    return (x - m) / jnp.sqrt(v + eps)

def _scatter_add(tgt, idx, src, axis=0):
    return tgt.at[idx].add(src)

def _segment_sum(src, seg, n):
    return jax.ops.segment_sum(src, seg, n)
kernel_name = 'mk_gnn_preln_d2_gnn_r8_53c5c5'

def setup_inputs(seed: int=0):
    np.random.seed(seed)
    _w = jnp.asarray

    def _rec_inputs():
        import jax
        import jax.numpy as jnp
        _gk = jax.random.key(seed)
        x = -0.000202 + 1 * jax.random.normal(jax.random.fold_in(_gk, 1), (12500, 64), jnp.float32)
        _s = jax.random.randint(jax.random.fold_in(_gk, 2), (200000,), 0, 12500, jnp.int32)
        _d = jax.random.randint(jax.random.fold_in(_gk, 3), (200000,), 0, 12500, jnp.int32)
        _loop = jnp.arange(12500, dtype=jnp.int32)
        src = jnp.concatenate([_s, _d, _loop])
        dst = jnp.concatenate([_d, _s, _loop])
        _o = jnp.argsort(dst, stable=True)
        src = src[_o]
        dst = dst[_o]
        edge_type_65 = jax.random.randint(jax.random.fold_in(_gk, 13), (412500,), 0, 65, jnp.int32)
        return (x, src, dst, edge_type_65)
    x, src, dst, edge_type_65 = _rec_inputs()

    def _L0_gnn_setup():
        import jax, jax.numpy as jnp
        import numpy as np
        N_SRC = 12500
        N_DST = 12500
        N_EDGES = 200000
        D = 64
        key = jax.random.key(seed)
        k1, k2, k3 = jax.random.split(key, 3)
        src_emb = jax.random.normal(k1, (N_SRC, D), dtype=jnp.float32)
        edge_src = jax.random.randint(k2, (N_EDGES,), 0, N_SRC, dtype=jnp.int64)
        edge_dst = jax.random.randint(k3, (N_EDGES,), 0, N_DST, dtype=jnp.int64)
        return {'src_emb': src_emb, 'edge_src': edge_src, 'edge_dst': edge_dst, 'n_dst': N_DST}
    _L0_gnn_all = _L0_gnn_setup()
    _L0_gnn_in = {k: v for k, v in _L0_gnn_all.items() if k in ()}
    del _L0_gnn_all

    def _L1_gnn_setup():
        import jax, jax.numpy as jnp
        import numpy as np
        N, E, D, R, L = (6250, 75000, 64, 65, 2)

        def _rgcn_conv(x, src, dst, edge_type, W_r, W_root, b):
            n, d = x.shape
            r = W_r.shape[0]
            seg = dst * r + edge_type
            msg = x[src]
            agg = jax.ops.segment_sum(msg, seg, num_segments=n * r).reshape(n, r, d)
            cnt = jax.ops.segment_sum(jnp.ones((msg.shape[0],), x.dtype), seg, num_segments=n * r).reshape(n, r, 1)
            mean = agg / jnp.maximum(cnt, 1.0)
            out = jnp.einsum('nrd,rdk->nk', mean, W_r)
            return out + x @ W_root + b
        key = jax.random.key(seed)
        ks = jax.random.split(key, 10)
        x = jax.random.normal(ks[0], (N, D), dtype=jnp.float32)
        edge_index = jax.random.randint(ks[1], (2, E), 0, N, dtype=jnp.int64)
        edge_type = jax.random.randint(ks[2], (E,), 0, R, dtype=jnp.int64)
        s = 1.0 / np.sqrt(D)
        W = jax.random.normal(ks[3], (L, R, D, D), dtype=jnp.float32) * s
        root = jax.random.normal(ks[4], (L, D, D), dtype=jnp.float32) * s
        bias = jax.random.normal(ks[5], (L, D), dtype=jnp.float32) * 0.01
        res_W = jax.random.normal(ks[6], (L, D, D), dtype=jnp.float32) * s
        res_b = jax.random.normal(ks[7], (L, D), dtype=jnp.float32) * 0.01
        return {'x': x, 'edge_index': edge_index, 'edge_type': edge_type, 'W': W, 'root': root, 'bias': bias, 'res_W': res_W, 'res_b': res_b}
    _L1_gnn_all = _L1_gnn_setup()
    _L1_gnn_in = {k: v for k, v in _L1_gnn_all.items() if k in ('W', 'root', 'bias', 'res_W', 'res_b')}
    del _L1_gnn_all
    return {'x': x, 'src': src, 'dst': dst, 'edge_type_65': edge_type_65, 'L1_gnn_W': _L1_gnn_in['W'], 'L1_gnn_root': _L1_gnn_in['root'], 'L1_gnn_bias': _L1_gnn_in['bias'], 'L1_gnn_res_W': _L1_gnn_in['res_W'], 'L1_gnn_res_b': _L1_gnn_in['res_b']}

def reference(x, src, dst, edge_type_65, L1_gnn_W, L1_gnn_root, L1_gnn_bias, L1_gnn_res_W, L1_gnn_res_b):
    import jax
    import jax.numpy as jnp

    def _L0_gnn_ref(src_emb, edge_src, edge_dst, n_dst):
        import jax, jax.numpy as jnp
        import numpy as np
        N_SRC = 12500
        N_DST = 12500
        N_EDGES = 200000
        D = 64
        n_src = src_emb.shape[0]
        ones = jnp.ones(edge_src.shape[0], dtype=src_emb.dtype)
        out_deg = jax.ops.segment_sum(ones, edge_src, num_segments=n_src)
        in_deg = jax.ops.segment_sum(ones, edge_dst, num_segments=n_dst)
        src_norm = jnp.clip(out_deg, 1.0) ** (-0.5)
        dst_norm = jnp.clip(in_deg, 1.0) ** (-0.5)
        h_src = src_emb * src_norm[:, None]
        msgs = h_src[edge_src]
        agg = jax.ops.segment_sum(msgs, edge_dst, num_segments=n_dst)
        return agg * dst_norm[:, None]

    def _L1_gnn_ref(x, edge_index, edge_type, W, root, bias, res_W, res_b):
        import jax, jax.numpy as jnp
        import numpy as np
        N, E, D, R, L = (6250, 75000, 64, 65, 2)

        def _rgcn_conv(x, src, dst, edge_type, W_r, W_root, b):
            n, d = x.shape
            r = W_r.shape[0]
            seg = dst * r + edge_type
            msg = x[src]
            agg = jax.ops.segment_sum(msg, seg, num_segments=n * r).reshape(n, r, d)
            cnt = jax.ops.segment_sum(jnp.ones((msg.shape[0],), x.dtype), seg, num_segments=n * r).reshape(n, r, 1)
            mean = agg / jnp.maximum(cnt, 1.0)
            out = jnp.einsum('nrd,rdk->nk', mean, W_r)
            return out + x @ W_root + b
        src, dst = (edge_index[0], edge_index[1])
        h = x
        for l in range(W.shape[0]):
            conv = _rgcn_conv(h, src, dst, edge_type, W[l], root[l], bias[l])
            conv = jax.nn.relu(conv)
            res = jax.nn.relu(h @ res_W[l] + res_b[l])
            h = conv + res
        return h
    edge_index = jnp.stack([src, dst])
    h = jnp.maximum(_layernorm(x, axis=-1), 0.0)
    x = x + _L0_gnn_ref(h, src, dst, 12500)
    h = jnp.maximum(_layernorm(x, axis=-1), 0.0)
    x = x + _L1_gnn_ref(h, edge_index, edge_type_65, L1_gnn_W, L1_gnn_root, L1_gnn_bias, L1_gnn_res_W, L1_gnn_res_b)
    return x

_drawn_inputs = setup_inputs


def setup_inputs(seed=0):
    import zlib

    import numpy as np

    out = dict(_drawn_inputs(seed))
    spreads = {}
    factors = {'L1_gnn_bias': 8.0, 'L1_gnn_res_b': 23.448}
    for name, (base, spread) in spreads.items():
        noise = np.random.default_rng([zlib.crc32(name.encode()), seed]).standard_normal(out[name].shape)
        drawn = base * np.exp(spread * noise) if base else spread * noise
        out[name] = jnp.asarray(drawn.astype(out[name].dtype))
    for name, factor in factors.items():
        out[name] = (out[name] * factor).astype(out[name].dtype)
    return out
```

```python
import concourse.bass as bass
from concourse import mybir
from contextlib import ExitStack

P = 128


class Chain:

    def __init__(self, eng, sem):
        self.eng, self.sem, self.n, self.base = eng, sem, 0, 0

    def __call__(self, ins, wait_alone=None):
        self.n += 1
        ins.then_inc(self.sem, 1)
        if wait_alone:
            wait_alone(self.eng, self.sem, self.base + self.n)
        else:
            self.eng.wait_ge(self.sem, self.base + self.n)

    def enter(self, i, per):
        self.before, self.per = self.n, per
        self.base, self.n = i * per + self.before, 0

    def leave(self, rounds):
        assert self.n == self.per, (self.n, self.per)
        self.base, self.n = 0, self.before + rounds * self.per


def gnn_kernel(nc, N, E, R, D, x, src, dst, etype, W, root, bias, res_W, res_b,
               tile_base, iota_row, part_col, ident_in, out):
    f32, bf16, i32 = mybir.dt.float32, mybir.dt.bfloat16, mybir.dt.int32
    ALU, ACT, AX = mybir.AluOpType, mybir.ActivationFunctionType, mybir.AxisListType

    NB = -(-N // P)
    S = NB
    T = -(-E // (P * S))
    J = 3
    K = T // J
    HALF = (T + 1) // 2
    ET = S * T
    FULL = E // P
    REST = E - FULL * P
    CH = -(-(ET + T) // P)
    ETP = CH * P
    GW = D + R
    RX = R + 2
    YW = RX * D
    BANK = 512
    YC = -(-YW // BANK)
    SG = 3
    YG = -(-YC // SG)
    EPS = 1e-5
    assert T == J * K and S % 2 == 0 and NB * P * RX < 1 << 24

    ctx = ExitStack()
    with ctx:
        def sb(name, shape, dt):
            return ctx.enter_context(nc.sbuf_tensor(name, shape, dt))

        def pb(name):
            return ctx.enter_context(nc.psum_tensor(name, [P, BANK], f32))

        def sem(name):
            return ctx.enter_context(nc.semaphore(name))

        h0_table = nc.dram_tensor("h0_table", [NB * P, D], f32, kind="Internal").ap()
        y_table = [nc.dram_tensor(f"y_table{l}", [(NB + 1) * P * RX, D], f32, kind="Internal").ap()
                   for l in range(2)]
        rel_row = nc.dram_tensor("rel_row", [CH * P, P], bf16, kind="Internal").ap()
        dump = nc.dram_tensor("dump", [P, 2, 16], f32, kind="Internal").ap()
        y_rows = [t.rearrange("(n r) d -> n (r d)", r=RX) for t in y_table]

        x_sb = sb("x_sb", [P, NB + 1, D], f32)
        src_i = sb("src_i", [P, ETP], i32)
        dst_rel = sb("dst_rel", [P, ETP], bf16)
        type_b = sb("type_b", [P, ETP], bf16)
        w_sb = sb("w_sb", [P, ETP], f32)
        c_inv = sb("c_inv", [P, NB + 3, R], f32)
        rows = sb("rows", [P, J, K, GW], f32)
        onehot = sb("onehot", [P, 2, K, 2 * P], f32)
        onehot_t = sb("onehot_t", [P, 2, K * P], f32)
        rel_b = sb("rel_b", [P, 2, K * P], bf16)
        type_oh = sb("type_oh", [P, K, R], f32)
        ystage = sb("ystage", [P, 2, SG * BANK], f32)
        w_mat = sb("w_mat", [D, YW], f32)
        brow = sb("brow", [1, 3 * D], f32)
        ones = sb("ones", [1, P], f32)
        idx_st = sb("idx_st", [P, J, K], i32)
        iota = sb("iota", [P, 2 * P], bf16)
        iota_f = sb("iota_f", [P, 2 * P], f32)
        pcol = sb("pcol", [P, 2], f32)
        tbase = sb("tbase", [P, CH], f32)
        ident = sb("ident", [P, P], f32)
        zeros = sb("zeros", [P, GW], f32)
        eps = sb("eps", [P, 1], f32)
        rr = sb("rr", [P, 2, 2 * D], f32)
        h = sb("h", [P, D], f32)
        hT = sb("hT", [D, P], f32)
        agg = sb("agg", [P, D], f32)
        stats = sb("stats", [P, 6], f32)
        mv = sb("mv", [P, 2], f32)
        col = sb("col", [P, 4], f32)
        nrm = sb("nrm", [P, 4, NB + 1], f32)

        def flat(t):
            return t[:, :, :].rearrange("p a b -> p (a b)") if len(t.shape) == 3 \
                else t[:, :, :, :].rearrange("p a b c -> p (a b c)")

        raw_src = flat(onehot)[:, 0:ETP].bitcast(i32)
        raw_dst = flat(c_inv)[:, 0:ETP].bitcast(i32)
        raw_type = w_sb[:, :].bitcast(i32)
        f_src, f_dst, f_type = (flat(onehot)[:, 0:ETP], flat(c_inv)[:, 0:ETP], w_sb[:, :])
        rel_raw = flat(rows)[:, 0:ETP // 2].bitcast(bf16)
        lo_hi = w_sb[:, :].bitcast(bf16).rearrange("p (a t) -> p a t", a=2)
        hist_oh = flat(onehot_t).bitcast(bf16).rearrange("p (a k n) -> p a k n", a=2, k=K)
        xc = flat(c_inv)[:, 0:(NB + 1) * D].rearrange("p (b d) -> p b d", d=D)
        HB = (NB + 2) // 2
        sq = flat(onehot)[:, 0:HB * D].rearrange("p (b d) -> p b d", d=D)

        block_ps = [pb(f"block_ps{i}") for i in range(2)]
        y_ps = [pb(f"y_ps{i}") for i in range(2)]
        t_ps = pb("t_ps")
        look_ps = [pb(f"look_ps{i}") for i in range(2)]
        deg_ps = pb("deg_ps")

        loaded = {k: sem(f"{k}_loaded") for k in ("consts", "x", "src", "dst", "type")}
        fill = sem("fill")
        tr_done = sem("tr_done")
        tr_read = sem("tr_read")
        raw_f = sem("raw_f")
        rel_saved = sem("rel_saved")
        hist_ready = sem("hist_ready")
        hist_done = sem("hist_done")
        dve_step = sem("dve_step")
        act_step = sem("act_step")
        sq_in = sem("sq_in")
        sq_out = sem("sq_out")
        h0_ready = sem("h0_ready")
        h0_saved = sem("h0_saved")
        keys_ready = sem("keys_ready")
        w_loaded = [sem(f"w_loaded{l}") for l in range(2)]
        passed = sem("passed")
        out_ready = sem("out_ready")
        out_saved = sem("out_saved")
        gathered = [[sem(f"gathered{l}{j}") for j in range(J)] for l in range(3)]
        idx_staged = [sem(f"idx_staged{l}") for l in range(3)]
        onehot_ready = [sem(f"onehot_ready{l}") for l in range(3)]
        scaled = [sem(f"scaled{l}") for l in range(3)]
        agg_done = [sem(f"agg_done{l}") for l in range(3)]
        block_done = [sem(f"block_done{l}") for l in range(3)]
        block_read = [sem(f"block_read{l}") for l in range(3)]
        h_ready = [sem(f"h_ready{l}") for l in range(3)]
        hT_done = [sem(f"hT_done{l}") for l in range(2)]
        hT_ready = [sem(f"hT_ready{l}") for l in range(2)]
        y_done = [sem(f"y_done{l}") for l in range(2)]
        y_read = [sem(f"y_read{l}") for l in range(2)]
        y_saved = [[sem(f"y_saved{l}{k}") for k in range(2)] for l in range(2)]
        rr_loaded = [[sem(f"rr_loaded{l}{k}") for k in range(2)] for l in range(3)]
        relb_loaded = [sem(f"relb_loaded{k}") for k in range(2)]
        oht_ready = sem("oht_ready")
        look_done = sem("look_done")
        look_read = sem("look_read")

        block = ctx.enter_context(nc.Block())
        N_CONST = 4
        XF = N // P
        XR = N - XF * P
        EVAC = 4
        TG = -(-CH // EVAC)

        def y_cols(c):
            return min(BANK, YW - c * BANK)

        def group_cols(g):
            return min(SG * BANK, YW - g * SG * BANK)

        def wait_alone(eng, sem, value):
            eng.wait_ge(sem, value)
            eng.sem_inc(passed, 1)

        @block.sync
        def _(sp):
            for to, of in ((iota_f, iota_row), (pcol, part_col), (tbase, tile_base), (ident, ident_in)):
                sp.dma_start(to[:, :], of).then_inc(loaded["consts"], 16)
            sp.wait_ge(fill, 4)
            for name, raw, of in (("type", raw_type, etype), ("dst", raw_dst, dst), ("src", raw_src, src)):
                v = raw.rearrange("p (c e) -> p c e", e=P)
                c0 = FULL // P
                r0 = FULL - c0 * P
                sp.dma_start(v[:, 0:c0, :], of[0:c0 * P * P].rearrange("(c p e) -> p c e", p=P, e=P))\
                  .then_inc(loaded[name], 16)
                sp.dma_start(v[0:r0, c0, :], of[c0 * P * P:FULL * P].rearrange("(p e) -> p e", e=P))\
                  .then_inc(loaded[name], 16)
                sp.dma_start(v[r0:r0 + 1, c0, 0:REST], of[FULL * P:E].rearrange("(p e) -> p e", p=1))\
                  .then_inc(loaded[name], 16)
            sp.dma_start(x_sb[:, 1:XF + 1, :], x[0:XF * P, :].rearrange("(b p) d -> p b d", p=P))\
              .then_inc(loaded["x"], 16)
            sp.dma_start(x_sb[0:XR, XF + 1, :], x[XF * P:N, :]).then_inc(loaded["x"], 16)

            def load_weights(l):
                wv = w_mat[:, :].rearrange("d (r k) -> d r k", k=D)
                sp.dma_start(wv[:, 0:R, :], W[l].rearrange("r d k -> d r k")).then_inc(w_loaded[l], 16)
                sp.dma_start(wv[:, R, :], root[l]).then_inc(w_loaded[l], 16)
                sp.dma_start(wv[:, R + 1, :], res_W[l]).then_inc(w_loaded[l], 16)
                sp.dma_start(brow[:, D:2 * D], bias[l:l + 1, :]).then_inc(w_loaded[l], 16)
                sp.dma_start(brow[:, 2 * D:3 * D], res_b[l:l + 1, :]).then_inc(w_loaded[l], 16)

            load_weights(0)
            sp.wait_ge(raw_f, 2)
            sp.dma_start(rel_row.rearrange("(c p) e -> p c e", p=P),
                         rel_raw.rearrange("p (c e) -> p c e", e=P)).then_inc(rel_saved, 16)
            sp.wait_ge(h0_ready, 1)
            sp.dma_start(h0_table.rearrange("(b p) d -> p b d", p=P), xc[:, 1:NB + 1, :])\
              .then_inc(h0_saved, 16)

            def load_rr(l, s, par):
                sp.dma_start(rr[:, par, :], y_rows[l - 1][bass.ds(s * P, P), R * D:YW])\
                  .then_inc(rr_loaded[l][par], 16)

            def load_rel(m, slot):
                if isinstance(m, int):
                    of = rel_row[m * K:(m + 1) * K, :]
                else:
                    of = rel_row[bass.ds(m * K, K), :]
                sp.dma_start(rel_b[:, slot, :],
                             of.rearrange("k e -> (k e)").partition_broadcast(P))\
                  .then_inc(relb_loaded[slot], 16)

            def save_y(l, s, u):
                for g in range(YG):
                    slot = (YG * u + g) % 2
                    wait_alone(sp, y_read[l], s * YC + min(g * SG + SG, YC) + 1)
                    sp.dma_start(y_rows[l][bass.ds(s * P, P), g * SG * BANK:g * SG * BANK + group_cols(g)],
                                 ystage[:, slot, 0:group_cols(g)]).then_inc(y_saved[l][slot], 16)

            def all_y_saved(l):
                n = YG * (S + 1)
                for slot in range(2):
                    sp.wait_ge(y_saved[l][slot], 16 * ((n + 1 - slot) // 2 + 1))

            for l in range(3):
                if l < 2:
                    for slot in range(2):
                        sp.dma_start(dump[:, slot, :], ystage[:, slot, 0:16]).then_inc(y_saved[l][slot], 16)
                if l >= 1:
                    all_y_saved(l - 1)
                    if l == 1:
                        load_weights(1)
                    sp.dma_start(rr[:, 0, :], y_rows[l - 1][0:P, R * D:YW]).then_inc(rr_loaded[l][0], 16)
                if l == 1:
                    sp.wait_ge(rel_saved, 16)
                    for m in range(2):
                        load_rel(m, m)
                with sp.Fori(0, S // 2) as i:
                    for u in range(2):
                        s = i * 2 + u
                        if l == 1:
                            for d in range(2, 2 + J):
                                sp.wait_ge(oht_ready, s * J + d - 1)
                                load_rel(s * J + d, (J * u + d) % 2)
                        if l >= 1:
                            sp.wait_ge(h_ready[l], s + 1)
                            load_rr(l, s + 1, 1 - u)
                        if l < 2:
                            save_y(l, s, u)
                if l < 2:
                    save_y(l, S, S % 2)
            sp.wait_ge(out_ready, 1)
            sp.dma_start(out[0:XF * P, :].rearrange("(b p) d -> p b d", p=P), x_sb[:, 1:XF + 1, :])\
              .then_inc(out_saved, 16)
            sp.dma_start(out[XF * P:N, :], x_sb[0:XR, XF + 1, :]).then_inc(out_saved, 16)
            sp.wait_ge(out_saved, 32)

        @block.gpsimd
        def _(pool):
            pool.memset(w_sb[:, :].bitcast(i32), -1).then_inc(fill, 1)
            pool.memset(raw_dst, -1).then_inc(fill, 1)
            pool.memset(raw_src, -1).then_inc(fill, 1)
            pool.memset(flat(x_sb), 0.0).then_inc(fill, 1)
            pool.memset(zeros[:, :], 0.0).then_inc(fill, 1)
            pool.memset(eps[:, :], EPS).then_inc(fill, 1)
            pool.memset(ones[:, :], 1.0).then_inc(fill, 1)
            pool.memset(brow[:, 0:D], 0.0).then_inc(fill, 1)
            pool.memset(flat(ystage), 0.0).then_inc(fill, 1)
            for l in range(3):
                table = h0_table if l == 0 else y_table[l - 1]
                if l == 0:
                    pool.wait_ge(h0_saved, 16)
                    pool.wait_ge(rel_saved, 16)
                else:
                    n = YG * (S + 1)
                    for slot in range(2):
                        pool.wait_ge(y_saved[l - 1][slot], 16 * ((n + 1 - slot) // 2 + 1))
                with pool.Fori(0, S) as s:
                    for j in range(J):
                        q = s * J + j
                        wait_alone(pool, idx_staged[l], q + 1)
                        wait_alone(pool, agg_done[l], q + 1)
                        for k in range(K):
                            pool.indirect_dma_start(
                                out=rows[:, j, k, 0:D], out_offset=None, in_=table,
                                in_offset=bass.IndirectOffsetOnAxis(ap=idx_st[:, j, k:k + 1], axis=0))\
                                .then_inc(gathered[l][j], 16)

        @block.scalar
        def _(act):
            def root_of(n, dst_ap, src_ap, **more):
                act.wait_ge(sq_in, n)
                nc.scalar.activation(dst_ap, src_ap, ACT.Sqrt, **more).then_inc(sq_out, 1)

            act.wait_ge(fill, 9)
            root_of(1, nrm[:, 0, :], nrm[:, 0, :], bias=eps[:, :])
            root_of(2, nrm[:, 1, :], nrm[:, 1, :])

            def stage(l, s, j):
                q0 = s * T + j * K
                of = src_i[:, j * K:(j + 1) * K] if isinstance(s, int) else src_i[:, bass.ds(q0, K)]
                nc.scalar.activation(idx_st[:, j, :], of, ACT.Copy).then_inc(idx_staged[l], 1)

            def emit_y(l, s, u, i):
                act.wait_ge(hT_done[l], s + 1 + 1)
                nc.scalar.activation(hT[:, :], t_ps[0:D, 0:P], ACT.Relu if l == 0 else ACT.Copy)\
                  .then_inc(hT_ready[l], 1)
                for g in range(YG):
                    n = YG * u + g
                    act.wait_ge(y_saved[l][n % 2], (i * YG + n // 2 + 1) * 16)
                    for c in range(g * SG, min(g * SG + SG, YC)):
                        act.wait_ge(y_done[l], s * YC + c + 1)
                        o = (c - g * SG) * BANK
                        nc.scalar.activation(ystage[:, n % 2, o:o + y_cols(c)],
                                             y_ps[c % 2][:, 0:y_cols(c)], ACT.Copy).then_inc(y_read[l], 1)

            for l in range(3):
                act.wait_ge(keys_ready, 1 if l == 0 else 2)
                act.wait_ge(agg_done[l], J)
                for j in range(J):
                    stage(l, 0, j)
                if l < 2:
                    nc.scalar.activation(col[:, 3:4], eps[:, :], ACT.Copy).then_inc(y_read[l], 1)
                with act.Fori(0, S // 2) as i:
                    for u in range(2):
                        s = i * 2 + u
                        act.wait_ge(agg_done[l], s * J + 1 + J)
                        stage(l, s + 1, 0)
                        if l == 0:
                            root_of(s * 2 + 3, col[:, 1:2], col[:, 0:1])
                            root_of(s * 2 + 4, col[:, 2:3], mv[:, 1:2], bias=eps[:, :])
                        for j in range(1, J):
                            act.wait_ge(agg_done[l], s * J + j + 1 + J)
                            stage(l, s + 1, j)
                        if l < 2:
                            emit_y(l, s, u, i)
                if l == 0:
                    root_of(S * 2 + 3, col[:, 1:2], col[:, 0:1])
                    root_of(S * 2 + 4, col[:, 2:3], mv[:, 1:2], bias=eps[:, :])
                if l < 2:
                    emit_y(l, S, S % 2, S // 2)

        @block.tensor
        def _(pe):
            pe.wait_ge(loaded["consts"], 16 * N_CONST)
            pe.wait_ge(fill, 9)
            for a, of in enumerate((f_type, f_dst, f_src)):
                pe.wait_ge(raw_f, a + 1)
                for g in range(TG):
                    n = a * TG + g
                    if n >= 2:
                        pe.wait_ge(tr_read, n - 1)
                    for c in range(g * EVAC, min(g * EVAC + EVAC, CH)):
                        ins = nc.tensor.transpose(y_ps[n % 2][:, (c % EVAC) * P:(c % EVAC + 1) * P],
                                                  of[:, c * P:(c + 1) * P], ident[:, :])
                    ins.then_inc(tr_done, 1)

            nc.tensor.matmul(deg_ps[:, 0:NB], zeros[:, 0:P], zeros[:, 0:NB], start=True, stop=False)\
              .then_inc(hist_done, 2)
            with pe.Fori(0, ET // K // 2) as i:
                for v in range(2):
                    pe.wait_ge(hist_ready, i * 2 + v + 1)
                    for k in range(K):
                        ins = nc.tensor.matmul(deg_ps[:, 0:NB], hist_oh[:, v, k, 0:P],
                                               hist_oh[:, v, k, P:P + NB], start=False, stop=False)
                    ins.then_inc(hist_done, 1)
            nc.tensor.matmul(deg_ps[:, 0:NB], zeros[:, 0:P], zeros[:, 0:NB], start=False, stop=True)\
              .then_inc(hist_done, 1)

            def transform(l, s):
                wait_alone(pe, h_ready[l], s + 1 + 1)
                nc.tensor.transpose(t_ps[0:D, 0:P], h[:, :], ident[:, :]).then_inc(hT_done[l], 1)
                pe.wait_ge(hT_ready[l], s + 1)
                for c in range(YC):
                    pe.wait_ge(y_read[l], s * YC + max(c - 1, 0) + 1)
                    n = y_cols(c)
                    lastc = c == YC - 1
                    ins = nc.tensor.matmul(y_ps[c % 2][:, 0:n], hT[:, :], w_mat[:, c * BANK:c * BANK + n],
                                           start=True, stop=not lastc)
                    if lastc:
                        o = R * D - c * BANK
                        ins = nc.tensor.matmul(y_ps[c % 2][:, o:o + 2 * D], ones[:, :], brow[:, D:3 * D],
                                               start=False, stop=True)
                    ins.then_inc(y_done[l], 1)

            def lookup(q_base, jn, slot0):
                for k in range(K):
                    t = jn * K + k
                    at = slot0 + (1 if t >= HALF else 0)
                    o = look_ps[k // 7][:, (k % 7) * R:(k % 7 + 1) * R]
                    for a in range(2):
                        c = c_inv[:, at + a, :] if isinstance(at, int) else \
                            c_inv[:, bass.ds(at + a, 1), :].rearrange("p a r -> p (a r)")
                        ins = nc.tensor.matmul(o, onehot_t[:, a, k * P:(k + 1) * P], c,
                                               start=a == 0, stop=a == 1)
                ins.then_inc(look_done, 1)

            for l in range(3):
                width = GW if l == 0 else D
                if l < 2:
                    pe.wait_ge(w_loaded[l], 16 * 5)
                for b in range(2):
                    ins = nc.tensor.matmul(block_ps[b][:, 0:width], zeros[:, 0:P], zeros[:, 0:width],
                                           start=True, stop=False)
                ins.then_inc(agg_done[l], J)
                if l < 2:
                    nc.tensor.matmul(t_ps[:, 0:P], zeros[:, 0:P], zeros[:, 0:P], start=True, stop=True)\
                      .then_inc(hT_done[l], 1)
                if l == 1:
                    pe.wait_ge(oht_ready, 1)
                    lookup(0, 0, 0)
                with pe.Fori(0, S // 2) as i:
                    for u in range(2):
                        s = i * 2 + u
                        for j in range(J):
                            q = s * J + j
                            if l == 1:
                                pe.wait_ge(oht_ready, q + 2)
                                pe.wait_ge(look_read, q + 1)
                                lookup(0, (j + 1) % J, s + 1 if j == J - 1 else s)
                            pe.wait_ge(onehot_ready[l], q + 1)
                            if l == 0:
                                pe.wait_ge(gathered[l][j], (s + 1) * 16 * K)
                            else:
                                pe.wait_ge(scaled[l], q + 1)
                            for k in range(K):
                                t = j * K + k
                                banks = (1 - u, u) if t < HALF else (u, 1 - u)
                                if t == HALF:
                                    pe.wait_ge(block_read[l], s + 1)
                                for a, b in enumerate(banks):
                                    ins = nc.tensor.matmul(
                                        block_ps[b][:, 0:width],
                                        onehot[:, (J * u + j) % 2, k, a * P:(a + 1) * P],
                                        rows[:, j, k, 0:width],
                                        start=(t == HALF and a == 1), stop=(t == HALF - 1 and a == 0))
                                    if t == HALF - 1 and a == 0:
                                        ins.then_inc(block_done[l], 1)
                            ins.then_inc(agg_done[l], 1)
                        if l < 2:
                            transform(l, s)
                for b in (S % 2, 1 - S % 2):
                    ins = nc.tensor.matmul(block_ps[b][:, 0:width], zeros[:, 0:P], zeros[:, 0:width],
                                           start=False, stop=True)
                ins.then_inc(block_done[l], 1)
                if l < 2:
                    transform(l, S)
                pe.wait_ge(block_read[l], S + 1)

        @block.vector
        def _(dve):
            V = nc.vector
            step = Chain(dve, dve_step)
            dve.wait_ge(loaded["consts"], 16 * N_CONST)
            step(V.tensor_copy(iota[:, :], iota_f[:, :]))
            dve.wait_ge(loaded["type"], 48)
            V.tensor_copy(f_type, raw_type).then_inc(raw_f, 1)
            dve.wait_ge(loaded["dst"], 48)
            step(V.tensor_tensor(f_dst.rearrange("p (c e) -> p c e", e=P),
                                 raw_dst.rearrange("p (c e) -> p c e", e=P),
                                 tbase[:, :].unsqueeze(2).to_broadcast([P, CH, P]), ALU.subtract))
            V.tensor_copy(rel_raw, f_dst).then_inc(raw_f, 1)
            dve.wait_ge(loaded["src"], 48)
            V.tensor_copy(f_src, raw_src).then_inc(raw_f, 1)
            for a, to in enumerate((type_b, dst_rel, src_i)):
                for g in range(TG):
                    n = a * TG + g
                    c0, c1 = g * EVAC * P, min(g * EVAC + EVAC, CH) * P
                    dve.wait_ge(tr_done, n + 1)
                    V.tensor_copy(to[:, c0:c1], y_ps[n % 2][:, 0:c1 - c0]).then_inc(tr_read, 1)
            dve.wait_ge(tr_read, 3 * TG)
            tmp = flat(onehot)[:, 0:ETP].bitcast(i32)
            step(V.tensor_single_scalar(tmp, src_i[:, :], P - 1, ALU.bitwise_and))
            step(V.tensor_copy(lo_hi[:, 0, :], tmp))
            step(V.tensor_single_scalar(tmp, src_i[:, :], 7, ALU.arith_shift_right))
            step(V.tensor_copy(lo_hi[:, 1, :], tmp))
            V.tensor_scalar_max(src_i[:, :], src_i[:, :], 0.0).then_inc(keys_ready, 1)

            def bcast_iota(n, k):
                return iota[:, 0:n].unsqueeze(1).to_broadcast([P, k, n])

            def part(t, q, n):
                return t[:, bass.ds(q * K, K)].unsqueeze(2).to_broadcast([P, K, n])

            with dve.Fori(0, ET // K // 2) as i:
                for v in range(2):
                    q = i * 2 + v
                    dve.wait_ge(hist_done, q + 1)
                    V.tensor_tensor(hist_oh[:, v, :, 0:P], bcast_iota(P, K),
                                    lo_hi[:, 0, bass.ds(q * K, K)].unsqueeze(2).to_broadcast([P, K, P]),
                                    ALU.is_equal)
                    V.tensor_tensor(hist_oh[:, v, :, P:P + NB], bcast_iota(NB, K),
                                    lo_hi[:, 1, bass.ds(q * K, K)].unsqueeze(2).to_broadcast([P, K, NB]),
                                    ALU.is_equal).then_inc(hist_ready, 1)
            dve.wait_ge(hist_done, ET // K + 3)
            dve.wait_ge(loaded["x"], 32)
            step(V.tensor_reduce(nrm[:, 2, :], x_sb[:, :, :], AX.X, ALU.add))
            step(V.tensor_scalar(nrm[:, 2, :], nrm[:, 2, :], 1.0 / D, None, ALU.mult))

            def wide(a, b0=0, b1=NB + 1):
                return nrm[:, a, b0:b1].unsqueeze(2).to_broadcast([P, b1 - b0, D])

            step(V.tensor_tensor(xc, x_sb[:, :, :], wide(2), ALU.subtract))
            for b0 in range(0, NB + 1, HB):
                b1 = min(b0 + HB, NB + 1)
                step(V.tensor_tensor(sq[:, 0:b1 - b0, :], xc[:, b0:b1, :], xc[:, b0:b1, :], ALU.mult))
                step(V.tensor_reduce(nrm[:, 0, b0:b1], sq[:, 0:b1 - b0, :], AX.X, ALU.add))
            V.tensor_scalar(nrm[:, 0, :], nrm[:, 0, :], 1.0 / D, None, ALU.mult).then_inc(sq_in, 1)
            step(V.memset(nrm[:, 1, 0:1], 1.0))
            V.tensor_scalar_max(nrm[:, 1, 1:NB + 1], deg_ps[:, 0:NB], 1.0).then_inc(sq_in, 1)
            dve.wait_ge(sq_out, 2)
            step(V.tensor_tensor(nrm[:, 2, :], nrm[:, 0, :], nrm[:, 1, :], ALU.mult))
            step(V.reciprocal(nrm[:, 3, :], nrm[:, 2, :]))
            step(V.tensor_tensor(xc, xc, wide(3), ALU.mult))
            V.tensor_scalar_max(xc, xc, 0.0).then_inc(h0_ready, 1)
            dve.wait_ge(h0_saved, 16)
            dve.wait_ge(rel_saved, 16)
            step(V.memset(flat(c_inv), 1.0))

            def make_onehot(l, q, u, j):
                dve.wait_ge(agg_done[l], q + 2)
                ins = V.tensor_tensor(onehot[:, (J * u + j) % 2, :, :], bcast_iota(2 * P, K),
                                      part(dst_rel, q, 2 * P), ALU.is_equal)
                if l == 0:
                    ins = V.tensor_tensor(rows[:, j, :, D:GW], bcast_iota(R, K), part(type_b, q, R),
                                          ALU.is_equal)
                ins.then_inc(onehot_ready[l], 1)

            def finish_block0(s):
                at = s if isinstance(s, int) else None
                ps = block_ps[1 - (s % 2 if at is not None else s_par[0])]
                xs = x_sb[:, at, :] if at is not None else x_sb[:, bass.ds(s, 1), :].rearrange("p a d -> p (a d)")
                ci = c_inv[:, at, :] if at is not None else c_inv[:, bass.ds(s, 1), :].rearrange("p a d -> p (a d)")
                dve.wait_ge(block_done[0], s + 1)
                step(V.tensor_reduce(col[:, 0:1], ps[:, D:GW], AX.X, ALU.add))
                V.tensor_scalar_max(col[:, 0:1], col[:, 0:1], 1.0).then_inc(sq_in, 1)
                step(V.tensor_scalar_max(ci, ps[:, D:GW], 1.0))
                V.tensor_copy(agg[:, :], ps[:, 0:D]).then_inc(block_read[0], 1)
                step(V.reciprocal(ci, ci))
                dve.wait_ge(sq_out, s * 2 + 3)
                step(V.reciprocal(col[:, 1:2], col[:, 1:2]))
                step(V.scalar_tensor_tensor(xs, agg[:, :], col[:, 1:2], xs, ALU.mult, ALU.add), wait_alone)
                step(V.bn_stats(stats[:, :], xs), wait_alone)
                V.bn_aggr(mv[:, :], stats[:, :]).then_inc(sq_in, 1)
                dve.wait_ge(sq_out, s * 2 + 4)
                step(V.reciprocal(col[:, 2:3], col[:, 2:3]))
                dve.wait_ge(hT_done[0], s + 1)
                V.tensor_scalar(h[:, :], xs, mv[:, 0:1], col[:, 2:3], ALU.subtract, ALU.mult)\
                 .then_inc(h_ready[0], 1)

            def finish_block(l, s):
                at = s if isinstance(s, int) else None
                par = s % 2 if at is not None else s_par[0]
                ps = block_ps[1 - par]
                dve.wait_ge(block_done[l], s + 1)
                dve.wait_ge(rr_loaded[l][par], ((s - par) // 2 if at is not None else s_half[0]) * 16 + 16)
                step(V.tensor_scalar_max(rr[:, par, D:2 * D], rr[:, par, D:2 * D], 0.0))
                ins = V.tensor_tensor(agg[:, :], ps[:, 0:D], rr[:, par, 0:D], ALU.add)
                ins.then_inc(block_read[l], 1)
                dve.wait_ge(block_read[l], s + 1)
                ins = V.scalar_tensor_tensor(h[:, :], agg[:, :], 0.0, rr[:, par, D:2 * D], ALU.max, ALU.add)
                ins.then_inc(h_ready[l], 1)
                if l == 2:
                    dve.wait_ge(h_ready[l], s + 1 + 1)
                    xs = x_sb[:, at, :] if at is not None else \
                        x_sb[:, bass.ds(s, 1), :].rearrange("p a d -> p (a d)")
                    step(V.tensor_tensor(xs, xs, h[:, :], ALU.add))

            def make_onehot_t(m, slot, uses):
                dve.wait_ge(relb_loaded[slot], uses * 16)
                for a in range(2):
                    ins = V.tensor_scalar(onehot_t[:, a, :], rel_b[:, slot, :], pcol[:, a:a + 1], None, ALU.is_equal)
                ins.then_inc(oht_ready, 1)

            def read_lookup(m):
                to = part(type_b, m, R) if not isinstance(m, int) else \
                    type_b[:, m * K:(m + 1) * K].unsqueeze(2).to_broadcast([P, K, R])
                step(V.tensor_tensor(type_oh[:, :, :], bcast_iota(R, K), to, ALU.is_equal))
                dve.wait_ge(look_done, m + 1)
                for b, (k0, k1) in enumerate(((0, min(7, K)), (7, K))):
                    ins = V.tensor_tensor(type_oh[:, k0:k1, :],
                                          look_ps[b][:, 0:(k1 - k0) * R].rearrange("p (k r) -> p k r", r=R),
                                          type_oh[:, k0:k1, :], ALU.mult)
                ins.then_inc(look_read, 1)
                dve.wait_ge(look_read, m + 1)
                wv = w_sb[:, bass.ds(m * K, K)] if not isinstance(m, int) else w_sb[:, m * K:(m + 1) * K]
                step(V.tensor_reduce(wv, type_oh[:, :, :], AX.X, ALU.add))

            s_par, s_half = [0], [None]
            for l in range(3):
                if l == 1:
                    dve.wait_ge(idx_staged[0], J * (S + 1))
                    step(V.tensor_scalar(src_i[:, :], src_i[:, :], float(P), float(RX), ALU.add, ALU.mult))
                    V.tensor_tensor(src_i[:, :], src_i[:, :], type_b[:, :], ALU.add).then_inc(keys_ready, 1)
                V.tensor_copy(col[:, 0:1], eps[:, :]).then_inc(h_ready[l], 1)
                if l == 1:
                    make_onehot_t(0, 0, 1)
                    read_lookup(0)
                with dve.Fori(0, S // 2) as i:
                    s_half[0] = i
                    per = {0: 2 * 7, 1: 2 * (1 + 2 * J), 2: 2 * 2}[l]
                    step.enter(i, per)
                    for u in range(2):
                        s = i * 2 + u
                        s_par[0] = u
                        for j in range(J):
                            q = s * J + j
                            if l == 1:
                                m = J * u + j + 1
                                dve.wait_ge(look_done, q + 1)
                                make_onehot_t(q + 1, m % 2, i * J + (m // 2 + 1))
                            make_onehot(l, q, u, j)
                            if l == 1:
                                read_lookup(q + 1)
                            if l >= 1:
                                dve.wait_ge(gathered[l][j], (s + 1) * 16 * K)
                                V.tensor_tensor(rows[:, j, :, 0:D], rows[:, j, :, 0:D], part(w_sb, q, D),
                                                ALU.mult).then_inc(scaled[l], 1)
                            if j == 1:
                                finish_block0(s) if l == 0 else finish_block(l, s)
                    step.leave(S // 2)
                s_half[0] = None
                finish_block0(S) if l == 0 else finish_block(l, S)
            V.tensor_copy(col[:, 0:1], eps[:, :]).then_inc(out_ready, 1)


_NAMES = ["x", "src", "dst", "edge_type_65", "L1_gnn_W", "L1_gnn_root", "L1_gnn_bias", "L1_gnn_res_W",
          "L1_gnn_res_b"]


def layout(N, E):
    import numpy as np
    nb = -(-N // P)
    t = -(-E // (P * nb))
    ch = -(-(nb * t + t) // P)
    tile = np.arange(ch * P)
    base = P * (tile // t - 1 + (tile % t >= (t + 1) // 2))
    return {
        "tile_base": np.ascontiguousarray(base.reshape(ch, P).T.astype(np.float32)),
        "iota_row": np.tile(np.arange(2 * P, dtype=np.float32), (P, 1)),
        "part_col": np.arange(P, dtype=np.float32)[:, None] + np.array([[0, P]], np.float32),
        "ident_in": np.eye(P, dtype=np.float32),
    }


def kernel(**inputs):
    import numpy as _np
    import concourse.bacc as _bacc
    from concourse import mybir as _mybir
    from concourse.bass_utils import run_bass_kernel_spmd as _run

    nc = _bacc.Bacc("TRN2", target_bir_lowering=False, num_devices=1)
    arrays, args = {}, []
    N, D = inputs["x"].shape
    E = inputs["src"].shape[0]
    for name, a in [(n, inputs[n]) for n in _NAMES] + list(layout(N, E).items()):
        a = _np.ascontiguousarray(a)
        arrays[f"in_{name}"] = a
        args.append(nc.dram_tensor(f"in_{name}", a.shape, _mybir.dt.from_np(a.dtype), kind="ExternalInput").ap())
    args.append(nc.dram_tensor("out_0", (N, D), _mybir.dt.float32, kind="ExternalOutput").ap())
    gnn_kernel(nc, N, E, inputs["L1_gnn_W"].shape[1], D, *args)
    r = _run(nc, [arrays], core_ids=[0])
    return r.results[0]["out_0"]
```
